# Optimizing a Trainium2 kernel written in Bass

```python
import numpy as np
import jax
import jax.numpy as jnp

def _softmax(x, axis=-1):
    return jax.nn.softmax(x, axis=axis)

def _gelu(x):
    return jax.nn.gelu(x, approximate=True)

def _silu(x):
    return jax.nn.silu(x)

def _sigmoid(x):
    return jax.nn.sigmoid(x)

def _layernorm(x, axis=-1, eps=1e-05):
    m = jnp.mean(x, axis=axis, keepdims=True)
    v = jnp.var(x, axis=axis, keepdims=True)
    return (x - m) / jnp.sqrt(v + eps)

def _scatter_add(tgt, idx, src, axis=0):
    return tgt.at[idx].add(src)

def _segment_sum(src, seg, n):
    return jax.ops.segment_sum(src, seg, n)
kernel_name = 'mk_gnn_preln_d2_gnn_r8_438256'

def setup_inputs(seed: int=0):
    np.random.seed(seed)
    _w = jnp.asarray

    def _rec_inputs():
        import jax
        import jax.numpy as jnp
        _gk = jax.random.key(seed)
        x = -8.776e-05 + 1 * jax.random.normal(jax.random.fold_in(_gk, 1), (6250, 512), jnp.float32)
        _s = jax.random.randint(jax.random.fold_in(_gk, 2), (50000,), 0, 6250, jnp.int32)
        _d = jax.random.randint(jax.random.fold_in(_gk, 3), (50000,), 0, 6250, jnp.int32)
        _loop = jnp.arange(6250, dtype=jnp.int32)
        src = jnp.concatenate([_s, _d, _loop])
        dst = jnp.concatenate([_d, _s, _loop])
        _o = jnp.argsort(dst, stable=True)
        src = src[_o]
        dst = dst[_o]
        edge_type_4 = jax.random.randint(jax.random.fold_in(_gk, 12), (106250,), 0, 4, jnp.int32)
        return (x, src, dst, edge_type_4)
    x, src, dst, edge_type_4 = _rec_inputs()

    def _L0_gnn_setup():
        import jax, jax.numpy as jnp
        import numpy as np
        N = 1250
        E = 20000
        DIM = 512
        R = 4
        EPS = 1e-05

        def layer_norm(h, w, b):
            mu = jnp.mean(h, axis=-1, keepdims=True)
            var = jnp.mean((h - mu) ** 2, axis=-1, keepdims=True)
            return (h - mu) * jax.lax.rsqrt(var + EPS) * w + b
        key = jax.random.key(seed)
        ks = jax.random.split(key, 12)
        s = 0.02
        inp = {'x': jax.random.normal(ks[0], (N, DIM), dtype=jnp.float32), 'edge_index': jax.random.randint(ks[1], (2, E), 0, N, dtype=jnp.int64), 'edge_type': jax.random.randint(ks[2], (E,), 0, R, dtype=jnp.int64), 'self_W': jax.random.normal(ks[3], (DIM, DIM), dtype=jnp.float32) * s, 'self_b': jnp.zeros((DIM,), dtype=jnp.float32), 'rel_W': jax.random.normal(ks[4], (R, DIM, DIM), dtype=jnp.float32) * s, 'rel_b': jnp.zeros((R, DIM), dtype=jnp.float32), 'ln1_w': jnp.ones((DIM,), dtype=jnp.float32), 'ln1_b': jnp.zeros((DIM,), dtype=jnp.float32), 'W1': jax.random.normal(ks[5], (DIM, 2 * DIM), dtype=jnp.float32) * s, 'b1': jnp.zeros((2 * DIM,), dtype=jnp.float32), 'W2': jax.random.normal(ks[6], (2 * DIM, DIM), dtype=jnp.float32) * s, 'b2': jnp.zeros((DIM,), dtype=jnp.float32), 'ln2_w': jnp.ones((DIM,), dtype=jnp.float32), 'ln2_b': jnp.zeros((DIM,), dtype=jnp.float32)}
        return inp
    _L0_gnn_all = _L0_gnn_setup()
    _L0_gnn_in = {k: v for k, v in _L0_gnn_all.items() if k in ('self_W', 'self_b', 'rel_W', 'rel_b', 'ln1_w', 'ln1_b', 'W1', 'b1', 'W2', 'b2', 'ln2_w', 'ln2_b')}
    del _L0_gnn_all

    def _L1_gnn_setup():
        import jax, jax.numpy as jnp
        import numpy as np
        N_NODES = 6250
        N_EDGES = 100000
        IN_DIM = 512
        HIDDEN = 512
        HEADS = 4
        C_HEAD = HIDDEN // (2 * HEADS)
        NEG_SLOPE = 0.2
        BN_EPS = 1e-05

        def gat_conv(x, src, dst, W, att_src, att_dst, bias):
            N = x.shape[0]
            h = jnp.einsum('nd,dhc->nhc', x, W)
            a_s = jnp.sum(h * att_src, axis=-1)
            a_d = jnp.sum(h * att_dst, axis=-1)
            e = jax.nn.leaky_relu(a_s[src] + a_d[dst], NEG_SLOPE)
            m = jax.ops.segment_max(e, dst, num_segments=N)
            m = jnp.where(jnp.isfinite(m), m, 0.0)
            ex = jnp.exp(e - m[dst])
            denom = jax.ops.segment_sum(ex, dst, num_segments=N)
            alpha = ex / (denom[dst] + 1e-16)
            out = jax.ops.segment_sum(alpha[:, :, None] * h[src], dst, num_segments=N)
            return out.reshape(N, HEADS * C_HEAD) + bias
        key = jax.random.key(seed)
        ks = jax.random.split(key, 12)
        glorot = lambda k, shape, fan: jax.random.normal(k, shape, jnp.float32) * np.sqrt(2.0 / fan)
        inp = {'x': jax.random.normal(ks[0], (N_NODES, IN_DIM), jnp.float32), 'edge_index': jax.random.randint(ks[1], (2, N_EDGES), 0, N_NODES, dtype=jnp.int32).astype(jnp.int64), 'W_f': glorot(ks[2], (IN_DIM, HEADS, C_HEAD), IN_DIM), 'att_src_f': glorot(ks[3], (HEADS, C_HEAD), C_HEAD), 'att_dst_f': glorot(ks[4], (HEADS, C_HEAD), C_HEAD), 'bias_f': jnp.zeros((HEADS * C_HEAD,), jnp.float32), 'W_b': glorot(ks[5], (IN_DIM, HEADS, C_HEAD), IN_DIM), 'att_src_b': glorot(ks[6], (HEADS, C_HEAD), C_HEAD), 'att_dst_b': glorot(ks[7], (HEADS, C_HEAD), C_HEAD), 'bias_b': jnp.zeros((HEADS * C_HEAD,), jnp.float32), 'W_fuse': glorot(ks[8], (HIDDEN, HIDDEN), HIDDEN), 'b_fuse': jnp.zeros((HIDDEN,), jnp.float32), 'bn_gamma': jnp.ones((HIDDEN,), jnp.float32), 'bn_beta': jnp.zeros((HIDDEN,), jnp.float32)}
        return inp
    _L1_gnn_all = _L1_gnn_setup()
    _L1_gnn_in = {k: v for k, v in _L1_gnn_all.items() if k in ('W_f', 'att_src_f', 'att_dst_f', 'bias_f', 'W_b', 'att_src_b', 'att_dst_b', 'bias_b', 'W_fuse', 'b_fuse', 'bn_gamma', 'bn_beta')}
    del _L1_gnn_all
    return {'x': x, 'src': src, 'dst': dst, 'edge_type_4': edge_type_4, 'L0_gnn_self_W': _L0_gnn_in['self_W'], 'L0_gnn_self_b': _L0_gnn_in['self_b'], 'L0_gnn_rel_W': _L0_gnn_in['rel_W'], 'L0_gnn_rel_b': _L0_gnn_in['rel_b'], 'L0_gnn_ln1_w': _L0_gnn_in['ln1_w'], 'L0_gnn_ln1_b': _L0_gnn_in['ln1_b'], 'L0_gnn_W1': _L0_gnn_in['W1'], 'L0_gnn_b1': _L0_gnn_in['b1'], 'L0_gnn_W2': _L0_gnn_in['W2'], 'L0_gnn_b2': _L0_gnn_in['b2'], 'L0_gnn_ln2_w': _L0_gnn_in['ln2_w'], 'L0_gnn_ln2_b': _L0_gnn_in['ln2_b'], 'L1_gnn_W_f': _L1_gnn_in['W_f'], 'L1_gnn_att_src_f': _L1_gnn_in['att_src_f'], 'L1_gnn_att_dst_f': _L1_gnn_in['att_dst_f'], 'L1_gnn_bias_f': _L1_gnn_in['bias_f'], 'L1_gnn_W_b': _L1_gnn_in['W_b'], 'L1_gnn_att_src_b': _L1_gnn_in['att_src_b'], 'L1_gnn_att_dst_b': _L1_gnn_in['att_dst_b'], 'L1_gnn_bias_b': _L1_gnn_in['bias_b'], 'L1_gnn_W_fuse': _L1_gnn_in['W_fuse'], 'L1_gnn_b_fuse': _L1_gnn_in['b_fuse'], 'L1_gnn_bn_gamma': _L1_gnn_in['bn_gamma'], 'L1_gnn_bn_beta': _L1_gnn_in['bn_beta']}

def reference(x, src, dst, edge_type_4, L0_gnn_self_W, L0_gnn_self_b, L0_gnn_rel_W, L0_gnn_rel_b, L0_gnn_ln1_w, L0_gnn_ln1_b, L0_gnn_W1, L0_gnn_b1, L0_gnn_W2, L0_gnn_b2, L0_gnn_ln2_w, L0_gnn_ln2_b, L1_gnn_W_f, L1_gnn_att_src_f, L1_gnn_att_dst_f, L1_gnn_bias_f, L1_gnn_W_b, L1_gnn_att_src_b, L1_gnn_att_dst_b, L1_gnn_bias_b, L1_gnn_W_fuse, L1_gnn_b_fuse, L1_gnn_bn_gamma, L1_gnn_bn_beta):
    import jax
    import jax.numpy as jnp

    def _L0_gnn_ref(x, edge_index, edge_type, self_W, self_b, rel_W, rel_b, ln1_w, ln1_b, W1, b1, W2, b2, ln2_w, ln2_b):
        import jax, jax.numpy as jnp
        import numpy as np
        N = 1250
        E = 20000
        DIM = 512
        R = 4
        EPS = 1e-05

        def layer_norm(h, w, b):
            mu = jnp.mean(h, axis=-1, keepdims=True)
            var = jnp.mean((h - mu) ** 2, axis=-1, keepdims=True)
            return (h - mu) * jax.lax.rsqrt(var + EPS) * w + b
        n = x.shape[0]
        src, dst = (edge_index[0], edge_index[1])
        h_all = jnp.einsum('nd,rdf->nrf', x, rel_W) + rel_b
        msg = h_all[src, edge_type]
        agg = jax.ops.segment_sum(msg, dst, num_segments=n)
        deg = jax.ops.segment_sum(jnp.ones_like(dst, dtype=x.dtype), dst, num_segments=n)
        agg = agg / jnp.maximum(deg, 1.0)[:, None]
        h = x @ self_W + self_b + agg
        x1 = layer_norm(x + h, ln1_w, ln1_b)
        f = jax.nn.gelu(x1 @ W1 + b1, approximate=False) @ W2 + b2
        out = layer_norm(x1 + f, ln2_w, ln2_b)
        return out

    def _L1_gnn_ref(x, edge_index, W_f, att_src_f, att_dst_f, bias_f, W_b, att_src_b, att_dst_b, bias_b, W_fuse, b_fuse, bn_gamma, bn_beta):
        import jax, jax.numpy as jnp
        import numpy as np
        N_NODES = 6250
        N_EDGES = 100000
        IN_DIM = 512
        HIDDEN = 512
        HEADS = 4
        C_HEAD = HIDDEN // (2 * HEADS)
        NEG_SLOPE = 0.2
        BN_EPS = 1e-05

        def gat_conv(x, src, dst, W, att_src, att_dst, bias):
            N = x.shape[0]
            h = jnp.einsum('nd,dhc->nhc', x, W)
            a_s = jnp.sum(h * att_src, axis=-1)
            a_d = jnp.sum(h * att_dst, axis=-1)
            e = jax.nn.leaky_relu(a_s[src] + a_d[dst], NEG_SLOPE)
            m = jax.ops.segment_max(e, dst, num_segments=N)
            m = jnp.where(jnp.isfinite(m), m, 0.0)
            ex = jnp.exp(e - m[dst])
            denom = jax.ops.segment_sum(ex, dst, num_segments=N)
            alpha = ex / (denom[dst] + 1e-16)
            out = jax.ops.segment_sum(alpha[:, :, None] * h[src], dst, num_segments=N)
            return out.reshape(N, HEADS * C_HEAD) + bias
        src, dst = (edge_index[0], edge_index[1])
        fwd = gat_conv(x, src, dst, W_f, att_src_f, att_dst_f, bias_f)
        bwd = gat_conv(x, dst, src, W_b, att_src_b, att_dst_b, bias_b)
        combined = jnp.concatenate([fwd, bwd], axis=1)
        fused = combined @ W_fuse + b_fuse
        mean = jnp.mean(fused, axis=0)
        var = jnp.mean(jnp.square(fused - mean), axis=0)
        normed = (fused - mean) * jax.lax.rsqrt(var + BN_EPS) * bn_gamma + bn_beta
        return jax.nn.relu(normed)
    edge_index = jnp.stack([src, dst])
    h = jnp.maximum(_layernorm(x, axis=-1), 0.0)
    x = x + _L0_gnn_ref(h, edge_index, edge_type_4, L0_gnn_self_W, L0_gnn_self_b, L0_gnn_rel_W, L0_gnn_rel_b, L0_gnn_ln1_w, L0_gnn_ln1_b, L0_gnn_W1, L0_gnn_b1, L0_gnn_W2, L0_gnn_b2, L0_gnn_ln2_w, L0_gnn_ln2_b)
    h = jnp.maximum(_layernorm(x, axis=-1), 0.0)
    x = x + _L1_gnn_ref(h, edge_index, L1_gnn_W_f, L1_gnn_att_src_f, L1_gnn_att_dst_f, L1_gnn_bias_f, L1_gnn_W_b, L1_gnn_att_src_b, L1_gnn_att_dst_b, L1_gnn_bias_b, L1_gnn_W_fuse, L1_gnn_b_fuse, L1_gnn_bn_gamma, L1_gnn_bn_beta)
    return x

_drawn_inputs = setup_inputs


def setup_inputs(seed=0):
    import zlib

    import numpy as np

    out = dict(_drawn_inputs(seed))
    spreads = {'L0_gnn_self_b': (0.0, 0.1),
     'L0_gnn_rel_b': (0.0, 0.1),
     'L0_gnn_ln1_w': (1.0, 0.2),
     'L0_gnn_ln1_b': (0.0, 0.1),
     'L0_gnn_b1': (0.0, 0.404),
     'L0_gnn_b2': (0.0, 0.1),
     'L0_gnn_ln2_w': (1.0, 0.2),
     'L0_gnn_ln2_b': (0.0, 0.1),
     'L1_gnn_bias_f': (0.0, 0.8),
     'L1_gnn_bias_b': (0.0, 0.8),
     'L1_gnn_b_fuse': (0.0, 0.8),
     'L1_gnn_bn_gamma': (1.0, 0.2),
     'L1_gnn_bn_beta': (0.0, 0.1)}
    factors = {}
    for name, (base, spread) in spreads.items():
        noise = np.random.default_rng([zlib.crc32(name.encode()), seed]).standard_normal(out[name].shape)
        drawn = base * np.exp(spread * noise) if base else spread * noise
        out[name] = jnp.asarray(drawn.astype(out[name].dtype))
    for name, factor in factors.items():
        out[name] = (out[name] * factor).astype(out[name].dtype)
    return out
```

```python
from contextlib import ExitStack

import concourse.bass as bass
from concourse import mybir

ALU = mybir.AluOpType
ACT = mybir.ActivationFunctionType
F32 = mybir.dt.float32
I32 = mybir.dt.int32
AX = mybir.AxisListType

P = 128
N = 6250
E = 106250
D = 512
R = 4
KD = D // P
FF = 2 * D
KF = FF // P
H = 4
C = D // (2 * H)
NB = (N + P - 1) // P
NPAD = NB * P
LAST = N - (NB - 1) * P
EC = 832
SG = 2
SE = SG * P
NG = (E + NB * (SE - 1)) // SE
NTILE = NG * SG
SLOTS = NTILE * P
HW = C + 1
TW = H * HW
ROW = TW + H
LN_EPS = 1e-5
BN_EPS = 1e-5
SLOPE = 0.2
TYPE_BITS = 2
LOCAL_BITS = 7
NODE_MASK = 0x1FFF
EMPTY = 1 << 23


def run_steps(eng, total, unroll, lag, step):
    for k in range(unroll):
        step(k, k, 0)
    rounds = (total - unroll) // unroll
    with eng.Fori(0, rounds) as j:
        for u in range(unroll):
            step(j * unroll + (unroll + u), u, j + 1)
    for k in range(unroll * (rounds + 1), total + lag):
        step(k, k % unroll, k // unroll)




def live(k, total):
    return not isinstance(k, int) or 0 <= k < total


def reused(k, ring):
    return not isinstance(k, int) or k >= ring


def program(nc, a):
    x, out = a["x"], a["out"]
    with ExitStack() as whole:
        def dram(name, shape, dt=F32):
            return nc.dram_tensor(name, shape, dt, kind=a["scratch_kind"]).ap()

        rel_rows = dram("rel_rows", (NPAD * R, D))
        base_rows = dram("base_rows", (NPAD, D))
        mid_rows = dram("mid_rows", (NPAD, D))
        gat_rows = [dram(f"gat_rows{d}", (NPAD, ROW)) for d in range(2)]
        slot_recs = [dram(f"slot_recs{d}", (SLOTS + EC, 1), I32) for d in range(2)]

        names = set()

        def sems(ctx, text):
            got = []
            for n in text.split():
                assert n not in names, n
                names.add(n)
                got.append(ctx.enter_context(nc.semaphore(n)))
            return got

        def sb(ctx, name, shape, dt=F32):
            return ctx.enter_context(nc.sbuf_tensor(name, shape, dt))

        def ps(ctx, name, shape, dt=F32):
            return ctx.enter_context(nc.psum_tensor(name, shape, dt))

        ident = sb(whole, "ident", [P, P])
        ones = sb(whole, "ones", [P, P])
        ones_last = sb(whole, "ones_last", [P, P])
        iota_row = sb(whole, "iota_row", [P, P])
        eps_col = sb(whole, "eps_col", [P, 1])
        group_block = sb(whole, "group_block", [P, 2, NG], I32)
        send_back = sb(whole, "send_back", [P, EC, 2], I32)
        aS = sb(whole, "aS", [P, 2, NB, H])
        aD = sb(whole, "aD", [P, 2, NB, H])

        sort_and_project(nc, a, dict(locals()))
        with ExitStack() as sums:
            acc = sb(sums, "acc", [P, NB * 2 * TW])
            relational_edges(nc, a, dict(locals()))
            relational_nodes(nc, a, dict(locals()))
            node_idx = [sb(sums, f"node_idx{d}", [P, NTILE], I32) for d in range(2)]
            local = [sb(sums, f"local{d}", [P, NTILE]) for d in range(2)]
            gat_scores(nc, a, dict(locals()))
            for d in range(2):
                gat_edges(nc, a, dict(locals()))
            fuse(nc, a, dict(locals()))


def scatter_records(nc, pool, d, send, slot_recs, stage, s_stage, s_sent):
    K = 8
    assert EC % (2 * K) == 0

    def step(k, half, r):
        if reused(k, 2):
            pool.wait_ge(s_sent[half], r * (16 * K))
            pool.nop(nofuse=True)
        nc.gpsimd.tensor_copy(stage[:, half], send[:, bass.ds(k * K, K), :]).then_inc(s_stage, 1)
        pool.wait_ge(s_stage, k + 1)
        pool.nop(nofuse=True)
        for c in range(K):
            nc.gpsimd.indirect_dma_start(
                out=slot_recs, out_offset=bass.IndirectOffsetOnAxis(ap=stage[:, half, c, 0:1], axis=0),
                in_=stage[:, half, c, 1:2], in_offset=None).then_inc(s_sent[half], 16)

    run_steps(pool, EC // K, 2, 0, step)
    for half in range(2):
        pool.wait_ge(s_sent[half], EC // 2 * 16)


def sort_and_project(nc, a, g):
    ident, ones, iota_row, eps_col = g["ident"], g["ones"], g["iota_row"], g["eps_col"]
    ones_last, group_block = g["ones_last"], g["group_block"]
    sb, ps, sems = g["sb"], g["ps"], g["sems"]
    slot_recs = g["slot_recs"]
    with ExitStack() as ctx:
        send = [sb(ctx, "send", [P, EC, 2], I32), g["send_back"]]
        edge = sb(ctx, "edge", [P, 3, EC], I32)
        lower = sb(ctx, "lower", [P, P])
        ones_row = sb(ctx, "ones_row", [P, EC])
        spare = sb(ctx, "spare", [P, EC], I32)
        key_block = sb(ctx, "key_block", [P, EC])
        key_int = sb(ctx, "key_int", [P, EC], I32)
        is_block = sb(ctx, "is_block", [P, EC])
        running = sb(ctx, "running", [P, EC])
        slot = sb(ctx, "slot", [P, EC])
        slot_int = sb(ctx, "slot_int", [P, EC], I32)
        slot_lo = sb(ctx, "slot_lo", [P, EC], I32)
        counts = sb(ctx, "counts", [P, NB])
        totals = sb(ctx, "totals", [P, NB])
        totals_int = sb(ctx, "totals_int", [P, NB], I32)
        groups = sb(ctx, "groups", [P, NB])
        group_end = sb(ctx, "group_end", [P, NB])
        first_slot = sb(ctx, "first_slot", [P, NB])
        group_iota = sb(ctx, "group_iota", [P, NG])
        group_of = sb(ctx, "group_of", [P, NG])
        empty = sb(ctx, "empty", [P, NTILE], I32)
        stage = sb(ctx, "stageA", [P, 2, 8, 2], I32)
        w = sb(ctx, "wA", [P, KD, (R + 1) * D])
        bias = sb(ctx, "biasA", [P, (R + 1) * D])
        xin = sb(ctx, "xinA", [P, 2, D])
        stats = sb(ctx, "statsA", [P, 2, 6])
        mv = sb(ctx, "mvA", [P, 2, 2])
        sd = sb(ctx, "sdA", [P, 2])
        rstd = sb(ctx, "rstdA", [P, 2])
        shift = sb(ctx, "shiftA", [P, 2])
        h = sb(ctx, "hA", [P, 2, D])
        hT = sb(ctx, "hTA", [P, 2, D])
        o = sb(ctx, "oA", [P, 2, (R + 1) * D])
        p_small = ps(ctx, "p_small", [P, 512])
        p_t = ps(ctx, "p_tA", [P, 512])
        p_o = ps(ctx, "p_oA", [P, R + 1, 512])

        (s_const, s_edge, s_w, s_chain, s_counts, s_prefix, s_send, s_empty_ready, s_empty,
         s_stage, s_sent0, s_sent1, s_block) = sems(
            ctx, "a_const a_edge a_w a_chain a_counts a_prefix a_send a_empty_ready a_empty "
                 "a_stage a_sent0 a_sent1 a_block")
        (s_x0, s_x1, s_stats, s_mv, s_sd, s_rstd, s_shift, s_h, s_t, s_hT, s_o, s_copied, s_base,
         s_rel0, s_rel1, s_out0, s_out1) = sems(
            ctx, "a_x0 a_x1 a_stats a_mv a_sd a_rstd a_shift a_h a_t a_hT a_o a_copied a_base "
                 "a_rel0 a_rel1 a_out0 a_out1")
        s_x = [s_x0, s_x1]
        s_rel_out, s_base_out = [s_rel0, s_rel1], [s_out0, s_out1]
        NCONST = 9
        block = ctx.enter_context(nc.Block())

        @block.gpsimd
        def _(pool):
            G = nc.gpsimd
            G.memset(ident[:], 0.0).then_inc(s_const, 1)
            G.memset(ones[:], 1.0).then_inc(s_const, 1)
            G.memset(lower[:], 0.0).then_inc(s_const, 1)
            pool.wait_ge(s_const, 3)
            G.affine_select(out=ident[:], in_=ident[:], compare_op=ALU.not_equal, fill=1.0, base=0,
                            pattern=[[-1, P]], channel_multiplier=1).then_inc(s_const, 1)
            G.affine_select(out=lower[:], in_=lower[:], compare_op=ALU.is_ge, fill=1.0, base=0,
                            pattern=[[-1, P]], channel_multiplier=1).then_inc(s_const, 1)
            G.affine_select(out=ones_last[:], in_=ones[:], compare_op=ALU.is_ge, fill=0.0, base=LAST - 1,
                            pattern=[[0, P]], channel_multiplier=-1).then_inc(s_const, 1)
            G.iota(iota_row[:], [[1, P]], base=0, channel_multiplier=0,
                   allow_small_or_imprecise_dtypes=True).then_inc(s_const, 1)
            G.iota(group_iota[:], [[1, NG]], base=0, channel_multiplier=0,
                   allow_small_or_imprecise_dtypes=True).then_inc(s_const, 1)
            G.iota(spare[:], [[1, EC]], base=SLOTS, channel_multiplier=0).then_inc(s_const, 1)
            pool.wait_ge(s_send, 1)
            pool.wait_ge(s_empty, 32)
            scatter_records(nc, pool, 0, send[0], slot_recs[0], stage, s_stage, [s_sent0, s_sent1])

        @block.sync
        def _(sp):
            for i, name in enumerate(("src", "dst", "edge_type_4")):
                sp.dma_start(edge[:, i], a[name]).then_inc(s_edge, 16)
            for r in range(R):
                sp.dma_start(w[:, :, r * D:(r + 1) * D],
                             a["L0_gnn_rel_W"][r].rearrange("(k p) f -> p k f", p=P)).then_inc(s_w, 16)
            sp.dma_start(w[:, :, R * D:], a["L0_gnn_self_W"].rearrange("(k p) f -> p k f", p=P)).then_inc(s_w, 16)
            sp.dma_start(bias[:, 0:R * D], a["L0_gnn_rel_b"].rearrange("r f -> (r f)").partition_broadcast(P)).then_inc(s_w, 16)
            sp.dma_start(bias[:, R * D:], a["L0_gnn_self_b"].partition_broadcast(P)).then_inc(s_w, 16)
            sp.wait_ge(s_empty_ready, 1)
            for d in range(2):
                sp.dma_start(slot_recs[d][0:SLOTS].rearrange("(p t) c -> p (t c)", p=P), empty[:]).then_inc(s_empty, 16)

            def step(k, u, r):
                if reused(k, 2):
                    sp.wait_ge(s_base, k - 1)
                sp.dma_start(xin[:, u], x_rows(a["x"], k)).then_inc(s_x[u], 16)

            run_steps(sp, NB, 2, 0, step)
            for u in range(2):
                sp.wait_ge(s_rel_out[u], 16 * len(range(u, NB, 2)))
                sp.wait_ge(s_base_out[u], 16 * len(range(u, NB, 2)))

        @block.vector
        def _(dve):
            V = nc.vector
            chain = [0]

            def link(ins):
                chain[0] += 1
                ins.then_inc(s_chain, 1)
                dve.wait_ge(s_chain, chain[0])

            V.memset(eps_col[:], LN_EPS)
            V.memset(ones_row[:], 1.0)
            V.memset(empty[:], EMPTY).then_inc(s_empty_ready, 1)
            dve.wait_ge(s_const, NCONST)
            dve.wait_ge(s_edge, 48)
            for d in range(2):
                key, other = edge[:, 1 - d], edge[:, d]
                link(V.tensor_scalar(key_int[:], key, LOCAL_BITS, None, ALU.logical_shift_right))
                link(V.tensor_copy(key_block[:], key_int[:]))
                link(V.tensor_scalar(slot_lo[:], key, P - 1, None, ALU.bitwise_and))
                link(V.scalar_tensor_tensor(slot_int[:], edge[:, 2], float(P), slot_lo[:], ALU.mult, ALU.add))
                link(V.scalar_tensor_tensor(send[d][:, :, 1], other, float(R * P), slot_int[:], ALU.mult, ALU.add))
                base = 3 * NB * d + NB * d
                with dve.Fori(0, NB) as b:
                    V.tensor_scalar(is_block[:], key_block[:], iota_row[:, bass.ds(b, 1)], None, ALU.is_equal, ALU.add,
                                    accum_out=counts[:, bass.ds(b, 1)]).then_inc(s_block, 1)
                    dve.wait_ge(s_block, b + (base + 1))
                V.memset(slot[:], 0.0).then_inc(s_counts, 1)
                dve.wait_ge(s_prefix, d + 1)
                link(V.tensor_copy(totals_int[:], p_small[:, 64:64 + NB]))
                link(V.tensor_scalar(totals[:], totals_int[:], float(SE - 1), None, ALU.add))
                link(V.tensor_copy(totals_int[:], totals[:]))
                link(V.tensor_scalar(totals_int[:], totals_int[:], SE.bit_length() - 1, None, ALU.logical_shift_right))
                link(V.tensor_copy(groups[:], totals_int[:]))
                link(V.tensor_tensor_scan(group_end[:], ones[:, 0:NB], groups[:], 0.0, ALU.mult, ALU.add))
                link(V.tensor_tensor(first_slot[:], group_end[:], groups[:], ALU.subtract))
                link(V.tensor_scalar(first_slot[:], first_slot[:], float(SE), -1.0, ALU.mult, ALU.add))
                link(V.tensor_tensor(first_slot[:], first_slot[:], p_small[:, 0:NB], ALU.add))
                with dve.Fori(0, NB) as b:
                    V.tensor_scalar(is_block[:], key_block[:], iota_row[:, bass.ds(b, 1)], None,
                                    ALU.is_equal).then_inc(s_block, 1)
                    dve.wait_ge(s_block, b * 3 + (base + NB + 1))
                    V.tensor_tensor_scan(running[:], ones_row[:], is_block[:], first_slot[:, bass.ds(b, 1)],
                                         ALU.mult, ALU.add).then_inc(s_block, 1)
                    dve.wait_ge(s_block, b * 3 + (base + NB + 2))
                    dve.nop(nofuse=True)
                    V.copy_predicated(slot[:], is_block[:].bitcast(I32), running[:]).then_inc(s_block, 1)
                    dve.wait_ge(s_block, b * 3 + (base + NB + 3))
                link(V.tensor_copy(slot_int[:], slot[:]))
                link(V.tensor_scalar(slot_lo[:], slot_int[:], P - 1, None, ALU.bitwise_and))
                link(V.tensor_scalar(slot_int[:], slot_int[:], LOCAL_BITS, None, ALU.logical_shift_right))
                link(V.scalar_tensor_tensor(slot_int[:], slot_lo[:], float(NTILE), slot_int[:], ALU.mult, ALU.add))
                link(V.tensor_scalar(key_int[:], key_block[:], float(NB), None, ALU.is_ge))
                link(V.copy_predicated(slot_int[:], key_int[:], spare[:]))
                link(V.tensor_copy(send[d][:, :, 0], slot_int[:]))
                link(V.memset(group_of[:], 0.0))
                for b in range(NB - 1):
                    link(V.scalar_tensor_tensor(group_of[:], group_iota[:], group_end[:, b:b + 1], group_of[:],
                                                ALU.is_ge, ALU.add))
                V.tensor_copy(group_block[:, d], group_of[:]).then_inc(s_send, 1)

            dve.wait_ge(s_w, 16 * (R + 3))

            def step(k, u, r):
                if live(k, NB):
                    dve.wait_ge(s_x[u], r * 16 + 16)
                    if reused(k, 2):
                        dve.wait_ge(s_shift, k - 1)
                    V.bn_stats(stats[:, u], xin[:, u]).then_inc(s_stats, 1)
                    dve.wait_ge(s_stats, k + 1)
                    if reused(k, 2):
                        dve.wait_ge(s_h, k - 1)
                    dve.nop(nofuse=True)
                    V.bn_aggr(mv[:, u], stats[:, u]).then_inc(s_mv, 1)
                    dve.wait_ge(s_sd, k + 1)
                    V.reciprocal(rstd[:, u:u + 1], sd[:, u:u + 1]).then_inc(s_rstd, 1)
                    dve.wait_ge(s_rstd, k + 1)
                    V.scalar_tensor_tensor(shift[:, u:u + 1], mv[:, u, 0:1], -1.0, rstd[:, u:u + 1],
                                           ALU.mult, ALU.mult).then_inc(s_shift, 1)
                if live(k - 1, NB):
                    v = 1 - u
                    if reused(k - 1, 2):
                        dve.wait_ge(s_rel_out[v], 8 * (k - 1 - v))
                        dve.wait_ge(s_base_out[v], 8 * (k - 1 - v))
                    for i in range(R + 1):
                        dve.wait_ge(s_o, (k - 1) * (R + 1) + (i + 1))
                        V.tensor_tensor(o[:, v, i * D:(i + 1) * D], p_o[:, i], bias[:, i * D:(i + 1) * D],
                                        ALU.add).then_inc(s_copied, 1)
                    dve.wait_ge(s_copied, (k - 1) * (R + 1) + (R + 1))
                    V.tensor_tensor(o[:, v, R * D:], o[:, v, R * D:], h[:, v], ALU.add).then_inc(s_base, 1)

            run_steps(dve, NB, 2, 1, step)

        @block.scalar
        def _(act):
            act.wait_ge(s_counts, 1)
            act.wait_ge(s_w, 16 * (R + 3))

            def step(k, u, r):
                if live(k, NB):
                    act.wait_ge(s_mv, k + 1)
                    nc.scalar.activation(sd[:, u:u + 1], mv[:, u, 1:2], ACT.Sqrt, bias=eps_col[:]).then_inc(s_sd, 1)
                    act.wait_ge(s_shift, k + 1)
                    if reused(k, 2):
                        act.wait_ge(s_base, k - 1)
                    nc.scalar.activation(h[:, u], xin[:, u], ACT.Relu, scale=rstd[:, u:u + 1],
                                         bias=shift[:, u:u + 1]).then_inc(s_h, 1)
                    act.wait_ge(s_t, k + 1)
                    if reused(k, 2):
                        act.wait_ge(s_o, (k - 1) * (R + 1))
                    nc.scalar.copy(hT[:, u], p_t[:]).then_inc(s_hT, 1)
                if live(k - 1, NB):
                    v = 1 - u
                    act.wait_ge(s_copied, (k - 1) * (R + 1) + R)
                    act.dma_start(g["rel_rows"].rearrange("(n r) f -> n (r f)", r=R)[bass.ds((k - 1) * P, P)],
                                  o[:, v, 0:R * D]).then_inc(s_rel_out[v], 16)
                    act.wait_ge(s_base, k)
                    act.dma_start(g["base_rows"][bass.ds((k - 1) * P, P)], o[:, v, R * D:]).then_inc(s_base_out[v], 16)

            run_steps(act, NB, 2, 1, step)

        @block.tensor
        def _(pe):
            T = nc.tensor
            for d in range(2):
                pe.wait_ge(s_counts, d + 1)
                T.matmul(p_small[:, 0:NB], lower[:], counts[:], start=True, stop=True)
                T.matmul(p_small[:, 64:64 + NB], ones[:], counts[:], start=True, stop=True).then_inc(s_prefix, 1)
            pe.wait_ge(s_w, 16 * (R + 3))

            def step(k, u, r):
                if live(k, NB):
                    pe.wait_ge(s_h, k + 1)
                    if reused(k, 1):
                        pe.wait_ge(s_hT, k)
                    for c in range(KD):
                        t = T.transpose(p_t[:, c * P:(c + 1) * P], h[:, u, c * P:(c + 1) * P], ident[:])
                    t.then_inc(s_t, 1)
                if live(k - 1, NB):
                    v = 1 - u
                    pe.wait_ge(s_hT, k)
                    for i in range(R + 1):
                        if reused(k - 1, 1):
                            pe.wait_ge(s_copied, (k - 2) * (R + 1) + (i + 1))
                        for c in range(KD):
                            m = T.matmul(p_o[:, i], hT[:, v, c * P:(c + 1) * P], w[:, c, i * D:(i + 1) * D],
                                         start=(c == 0), stop=(c == KD - 1))
                        m.then_inc(s_o, 1)

            run_steps(pe, NB, 2, 1, step)


def x_rows(ap, k):
    return ap[bass.ds(k * P, P)]


def unpack(V, link, recs, scratch, idx, by_type, local):
    if by_type:
        link(V.tensor_scalar(idx[:], recs[:], LOCAL_BITS, NODE_MASK * R + R - 1,
                             ALU.logical_shift_right, ALU.bitwise_and))
    else:
        link(V.tensor_scalar(idx[:], recs[:], LOCAL_BITS + TYPE_BITS, NODE_MASK,
                             ALU.logical_shift_right, ALU.bitwise_and))
    link(V.tensor_scalar(scratch[:], recs[:], P - 1, None, ALU.bitwise_and))
    link(V.tensor_copy(local[:], scratch[:]))
    link(V.tensor_scalar(scratch[:], recs[:], EMPTY.bit_length() - 1, None, ALU.logical_shift_right))
    link(V.scalar_tensor_tensor(local[:], scratch[:], float(P), local[:], ALU.mult, ALU.add))


def relational_edges(nc, a, g):
    acc, group_block = g["acc"], g["group_block"]
    ones, iota_row = g["ones"], g["iota_row"]
    sb, ps, sems = g["sb"], g["ps"], g["sems"]
    RING, RP = 4, 2
    W1 = D + 1
    with ExitStack() as ctx:
        recs = sb(ctx, "recsB", [P, NTILE], I32)
        scratch = sb(ctx, "scratchB", [P, NTILE], I32)
        rel_idx = sb(ctx, "rel_idxB", [P, NTILE], I32)
        local = sb(ctx, "localB", [P, NTILE])
        stage = sb(ctx, "stageB", [P, RING, SG], I32)
        rows = [[sb(ctx, f"rowsB{i}{j}", [P, D]) for j in range(SG)] for i in range(RING)]
        hot = sb(ctx, "hotB", [P, RP, SG, P])
        p_sum = ps(ctx, "p_sumB", [P, RP, 1024])
        s_recs, s_chain, s_unpacked, s_hot, s_sum, s_add, s_stage = sems(
            ctx, "b_recs b_chain b_unpacked b_hot b_sum b_add b_stage")
        s_rows = sems(ctx, " ".join(f"b_rows{i}" for i in range(RING)))
        block = ctx.enter_context(nc.Block())

        @block.sync
        def _(sp):
            sp.dma_start(recs[:], g["slot_recs"][0][0:SLOTS].rearrange("(p t) c -> p (t c)", p=P)).then_inc(s_recs, 16)

        @block.scalar
        def _(act):
            act.wait_ge(s_unpacked, 1)

            def step(k, u, r):
                if reused(k, RING):
                    act.wait_ge(s_rows[u], r * (16 * SG))
                nc.scalar.copy(stage[:, u], rel_idx[:, bass.ds(k * SG, SG)]).then_inc(s_stage, 1)

            run_steps(act, NG, RING, 0, step)

        @block.gpsimd
        def _(pool):
            def step(k, u, r):
                pool.wait_ge(s_stage, k + 1)
                pool.nop(nofuse=True)
                if reused(k, RING):
                    pool.wait_ge(s_sum, k - (RING - 1))
                    pool.nop(nofuse=True)
                for j in range(SG):
                    nc.gpsimd.indirect_dma_start(
                        out=rows[u][j][:], out_offset=None, in_=g["rel_rows"],
                        in_offset=bass.IndirectOffsetOnAxis(ap=stage[:, u, j:j + 1], axis=0)).then_inc(s_rows[u], 16)

            run_steps(pool, NG, RING, 0, step)

        @block.vector
        def _(dve):
            V = nc.vector
            chain = [0]

            def link(ins):
                chain[0] += 1
                ins.then_inc(s_chain, 1)
                dve.wait_ge(s_chain, chain[0])

            dve.wait_ge(s_recs, 16)
            unpack(V, link, recs, scratch, rel_idx, True, local)
            V.memset(acc[:, 0:NB * W1], 0.0).then_inc(s_add, 1)
            V.memset(scratch[:], 0).then_inc(s_unpacked, 1)

            def step(k, u, r):
                if live(k, NG):
                    if reused(k, RP):
                        dve.wait_ge(s_sum, k - 1)
                    for j in range(SG):
                        V.tensor_scalar(hot[:, u % RP, j], iota_row[:], local[:, bass.ds(k * SG + j, 1)], None,
                                        ALU.is_equal).then_inc(s_hot, 1)
                if live(k - 1, NG):
                    b = dve.value_load(group_block[0:1, 0, bass.ds(k - 1, 1)], min_val=0, max_val=NB - 1)
                    dve.wait_ge(s_sum, k)
                    dve.wait_ge(s_add, k)
                    at = acc[:, bass.ds(b * W1, W1)]
                    V.tensor_tensor(at, at, p_sum[:, (u + 1) % RP, 0:W1], ALU.add).then_inc(s_add, 1)

            run_steps(dve, NG, RING, 1, step)

        @block.tensor
        def _(pe):
            T = nc.tensor

            def step(k, u, r):
                v = u % RP
                pe.wait_ge(s_hot, k * SG + SG)
                if reused(k, RP):
                    pe.wait_ge(s_add, k)
                pe.wait_ge(s_rows[u], r * (16 * SG) + 16 * SG)
                for j in range(SG):
                    T.matmul(p_sum[:, v, 0:D], hot[:, v, j], rows[u][j][:], start=(j == 0), stop=(j == SG - 1))
                    m = T.matmul(p_sum[:, v, D:W1], hot[:, v, j], ones[:, 0:1], start=(j == 0), stop=(j == SG - 1))
                m.then_inc(s_sum, 1)

            run_steps(pe, NG, RING, 0, step)


def relational_nodes(nc, a, g):
    acc, ident, eps_col = g["acc"], g["ident"], g["eps_col"]
    sb, ps, sems = g["sb"], g["ps"], g["sems"]
    W1C = D + 1
    W16 = 4 * H
    with ExitStack() as ctx:
        stage = sb(ctx, "stageC", [P, 2, 8, 2], I32)
        w1 = sb(ctx, "w1C", [P, KD, FF])
        w2 = sb(ctx, "w2C", [P, KF, D])
        wg = sb(ctx, "wgC", [P, KD, D])
        wa = sb(ctx, "waC", [P, KD, 2, 2 * H])
        rows = {n: sb(ctx, f"row_{n}", [P, D]) for n in ("ln1_w", "ln1_b", "ln2_w", "ln2_b", "b2")}
        b1 = sb(ctx, "b1C", [P, KF])
        xin = sb(ctx, "xinC", [P, 2, D])
        inv_deg = sb(ctx, "inv_degC", [P, 2])
        y = sb(ctx, "yC", [P, 2, D])
        yT = sb(ctx, "yTC", [P, 2, D])
        hid = sb(ctx, "hidC", [P, 2, KF * P])
        att, prod = hid[:, 0].rearrange("p (i f) -> p i f", i=2), hid[:, 1, 0:D]
        z = sb(ctx, "zC", [P, 2, D])
        n3 = sb(ctx, "n3C", [P, 2, D])
        n3T = sb(ctx, "n3TC", [P, 2, D])
        table = sb(ctx, "tableC", [P, 2, 2, ROW])
        stats = sb(ctx, "statsC", [P, 3, 6])
        mv = sb(ctx, "mvC", [P, 3, 2])
        sd = sb(ctx, "sdC", [P, 3])
        rstd = sb(ctx, "rstdC", [P, 3])
        shift = sb(ctx, "shiftC", [P, 3])
        p_t = ps(ctx, "p_tC", [P, 512])
        p_u = ps(ctx, "p_uC", [P, 2, 512])
        p_f = ps(ctx, "p_fC", [P, 2, 512])
        p_g = ps(ctx, "p_gC", [P, 2, 512])
        p_a = ps(ctx, "p_aC", [P, 512])
        (s_w, s_set, s_wa, s_chain, s_stage, s_sent0, s_sent1) = sems(
            ctx, "c_w c_set c_wa c_chain c_stage c_sent0 c_sent1")
        s_in = sems(ctx, "c_in0 c_in1")
        s_mid, s_tab = sems(ctx, "c_mid0 c_mid1"), sems(ctx, "c_tab0 c_tab1")
        (s_mv1, s_mv2, s_mv3, s_sd1, s_sd2, s_sd3, s_y, s_z, s_n3, s_t1, s_yT, s_u, s_hid, s_f, s_t3,
         s_n3T, s_g, s_tabled, s_score) = sems(
            ctx, "c_mv1 c_mv2 c_mv3 c_sd1 c_sd2 c_sd3 c_y c_z c_n3 c_t1 c_yT c_u c_hid c_f c_t3 "
                 "c_n3T c_g c_tabled c_score")
        s_own_a, s_own_b = sems(ctx, "c_own_a c_own_b")
        NA, NBB = 7, 11
        block = ctx.enter_context(nc.Block())

        @block.gpsimd
        def _(pool):
            scatter_records(nc, pool, 1, g["send_back"], g["slot_recs"][1], stage, s_stage, [s_sent0, s_sent1])

        @block.sync
        def _(sp):
            for n, ap in rows.items():
                sp.dma_start(ap[:], a["L0_gnn_" + n].partition_broadcast(P)).then_inc(s_w, 16)
            sp.dma_start(b1[:], a["L0_gnn_b1"]).then_inc(s_w, 16)
            sp.dma_start(w1[:], a["L0_gnn_W1"].rearrange("(k p) f -> p k f", p=P)).then_inc(s_w, 16)
            sp.dma_start(w2[:], a["L0_gnn_W2"].rearrange("(k p) f -> p k f", p=P)).then_inc(s_w, 16)
            for d, t in enumerate("fb"):
                cols = slice(d * H * C, (d + 1) * H * C)
                sp.dma_start(wg[:, :, cols], a["L1_gnn_W_" + t].rearrange("(k p) h c -> p k (h c)", p=P)).then_inc(s_w, 16)
                for i, end in enumerate(("src", "dst")):
                    sp.dma_start(att[:, i, cols], a[f"L1_gnn_att_{end}_{t}"].rearrange("h c -> (h c)").partition_broadcast(P)).then_inc(s_w, 16)

            def step(k, u, r):
                if reused(k, 2):
                    sp.wait_ge(s_z, k - 1)
                sp.dma_start(xin[:, u], x_rows(a["x"], k)).then_inc(s_in[u], 16)
                sp.dma_start(y[:, u], x_rows(g["base_rows"], k)).then_inc(s_in[u], 16)

            run_steps(sp, NB, 2, 0, step)

        @block.vector
        def _(dve):
            V = nc.vector
            chain = [0]

            def link(ins):
                chain[0] += 1
                ins.then_inc(s_chain, 1)
                dve.wait_ge(s_chain, chain[0])

            for u in range(2):
                for d in range(2):
                    V.memset(table[:, u, d, :], 1.0).then_inc(s_set, 1)
            dve.wait_ge(s_w, 16 * 14)
            for c in range(KD):
                for i in range(2):
                    link(V.tensor_tensor(prod, wg[:, c], att[:, i], ALU.mult))
                    link(V.tensor_reduce(wa[:, c, i], prod.rearrange("p (h c) -> p h c", c=C), AX.X, ALU.add))
            V.memset(prod, 0.0).then_inc(s_wa, 1)

            def own_a(ins, k, n):
                ins.then_inc(s_own_a, 1)
                dve.wait_ge(s_own_a, k * NA + n)

            def own_b(ins, k, n):
                ins.then_inc(s_own_b, 1)
                dve.wait_ge(s_own_b, k * NBB + n)

            def norm(src, i, k, s_mv, s_sd, own, first):
                own(V.bn_stats(stats[:, i], src), k, first)
                dve.nop(nofuse=True)
                V.bn_aggr(mv[:, i], stats[:, i]).then_inc(s_mv, 1)
                dve.wait_ge(s_sd, k + 1)
                own(V.reciprocal(rstd[:, i:i + 1], sd[:, i:i + 1]), k, first + 1)
                own(V.scalar_tensor_tensor(shift[:, i:i + 1], mv[:, i, 0:1], -1.0, rstd[:, i:i + 1],
                                           ALU.mult, ALU.mult), k, first + 2)

            def step(k, u, r):
                if live(k, NB):
                    dve.wait_ge(s_in[u], r * 32 + 32)
                    deg = acc[:, bass.ds(k * W1C + D, 1)]
                    own_a(V.tensor_scalar(inv_deg[:, u:u + 1], deg, 1.0, None, ALU.max), k, 1)
                    own_a(V.reciprocal(inv_deg[:, u:u + 1], inv_deg[:, u:u + 1]), k, 2)
                    own_a(V.scalar_tensor_tensor(y[:, u], acc[:, bass.ds(k * W1C, D)], inv_deg[:, u:u + 1], y[:, u],
                                               ALU.mult, ALU.add), k, 3)
                    norm(y[:, u], 0, k, s_mv1, s_sd1, own_a, 4)
                    own_a(V.tensor_scalar(y[:, u], y[:, u], rstd[:, 0:1], shift[:, 0:1], ALU.mult, ALU.add), k, 7)
                    V.tensor_tensor(y[:, u], y[:, u], rows["ln1_w"][:], ALU.mult).then_inc(s_y, 1)
                    dve.wait_ge(s_y, 2 * k + 1)
                    V.tensor_tensor(y[:, u], y[:, u], rows["ln1_b"][:], ALU.add).then_inc(s_y, 1)
                if live(k - 1, NB):
                    q, v = k - 1, 1 - u
                    dve.wait_ge(s_f, q + 1)
                    if reused(q, 2):
                        dve.wait_ge(s_mid[v], 8 * (q - v))
                    own_b(V.tensor_tensor(z[:, v], p_f[:, v], rows["b2"][:], ALU.add), q, 1)
                    own_b(V.tensor_tensor(z[:, v], z[:, v], y[:, v], ALU.add), q, 2)
                    norm(z[:, v], 1, q, s_mv2, s_sd2, own_b, 3)
                    own_b(V.tensor_scalar(z[:, v], z[:, v], rstd[:, 1:2], shift[:, 1:2], ALU.mult, ALU.add), q, 6)
                    own_b(V.tensor_tensor(z[:, v], z[:, v], rows["ln2_w"][:], ALU.mult), q, 7)
                    own_b(V.tensor_tensor(z[:, v], z[:, v], rows["ln2_b"][:], ALU.add), q, 8)
                    V.tensor_tensor(z[:, v], z[:, v], xin[:, v], ALU.add).then_inc(s_z, 1)
                    dve.wait_ge(s_z, q + 1)
                    if reused(q, 1):
                        dve.wait_ge(s_n3, q)
                    norm(z[:, v], 2, q, s_mv3, s_sd3, own_b, 9)
                if live(k - 2, NB):
                    q, v = k - 2, u
                    dve.wait_ge(s_g, q + 1)
                    dve.nop(nofuse=True)
                    for i, to in enumerate((g["aS"], g["aD"])):
                        V.tensor_copy(to[:, :, bass.ds(q, 1), :],
                                      p_a[:, i * 2 * H:(i + 1) * 2 * H].rearrange("p (d o h) -> p d o h", d=2, o=1)).then_inc(s_score, 1)

            run_steps(dve, NB, 2, 2, step)

        @block.scalar
        def _(act):
            S = nc.scalar
            act.wait_ge(s_w, 16 * 14)
            act.wait_ge(s_set, 4)

            def step(k, u, r):
                if live(k, NB):
                    act.wait_ge(s_mv1, k + 1)
                    S.activation(sd[:, 0:1], mv[:, 0, 1:2], ACT.Sqrt, bias=eps_col[:]).then_inc(s_sd1, 1)
                    act.wait_ge(s_t1, k + 1)
                    S.copy(yT[:, u], p_t[:]).then_inc(s_yT, 1)
                    for m in range(KF):
                        act.wait_ge(s_u, k * KF + (m // 4 * 4 + 4))
                        if reused(k, 2) and m == 0:
                            act.wait_ge(s_f, k - 1)
                        S.activation(hid[:, u, m * P:(m + 1) * P], p_u[:, m // 4, (m % 4) * P:(m % 4 + 1) * P],
                                     ACT.Gelu, bias=b1[:, m:m + 1]).then_inc(s_hid, 1)
                if live(k - 1, NB):
                    q, v = k - 1, 1 - u
                    act.wait_ge(s_mv2, k)
                    S.activation(sd[:, 1:2], mv[:, 1, 1:2], ACT.Sqrt, bias=eps_col[:]).then_inc(s_sd2, 1)
                    act.wait_ge(s_z, k)
                    act.dma_start(x_rows(g["mid_rows"], q), z[:, v]).then_inc(s_mid[v], 16)
                    act.wait_ge(s_mv3, k)
                    S.activation(sd[:, 2:3], mv[:, 2, 1:2], ACT.Sqrt, bias=eps_col[:]).then_inc(s_sd3, 1)
                    act.wait_ge(s_own_b, q * NBB + NBB)
                    if reused(q, 2):
                        act.wait_ge(s_t3, q - 1)
                    S.activation(n3[:, v], z[:, v], ACT.Relu, scale=rstd[:, 2:3], bias=shift[:, 2:3]).then_inc(s_n3, 1)
                    act.wait_ge(s_t3, k)
                    S.copy(n3T[:, v], p_t[:]).then_inc(s_n3T, 1)
                    act.wait_ge(s_g, k)
                    if reused(q, 2):
                        act.wait_ge(s_tab[v], 16 * (q - v))
                    for d in range(2):
                        S.copy(table[:, v, d, 0:TW].rearrange("p (h c) -> p h c", c=HW)[:, :, 0:C],
                               p_g[:, v, d * H * C:(d + 1) * H * C].rearrange("p (h c) -> p h c", c=C)).then_inc(s_tabled, 1)
                    act.wait_ge(s_tabled, 2 * k)
                    for d in range(2):
                        act.dma_start(x_rows(g["gat_rows"][d], q), table[:, v, d]).then_inc(s_tab[v], 16)

            run_steps(act, NB, 2, 1, step)
            for u in range(2):
                n = len(range(u, NB, 2))
                act.wait_ge(s_mid[u], 16 * n)
                act.wait_ge(s_tab[u], 32 * n)

        @block.tensor
        def _(pe):
            T = nc.tensor
            pe.wait_ge(s_w, 16 * 14)
            pe.wait_ge(s_wa, 1)

            def step(k, u, r):
                if live(k, NB):
                    pe.wait_ge(s_y, 2 * k + 2)
                    if reused(k, 2):
                        pe.wait_ge(s_n3T, k - 1)
                    for c in range(KD):
                        t = T.transpose(p_t[:, c * P:(c + 1) * P], y[:, u, c * P:(c + 1) * P], ident[:])
                    t.then_inc(s_t1, 1)
                    pe.wait_ge(s_yT, k + 1)
                    for m in range(KF):
                        if reused(k, 1):
                            pe.wait_ge(s_hid, (k - 1) * KF + (m // 4 * 4 + 4))
                        for c in range(KD):
                            i = T.matmul(p_u[:, m // 4, (m % 4) * P:(m % 4 + 1) * P], w1[:, c, m * P:(m + 1) * P],
                                         yT[:, u, c * P:(c + 1) * P], start=(c == 0), stop=(c == KD - 1))
                        i.then_inc(s_u, 1)
                    if reused(k, 2):
                        pe.wait_ge(s_z, k - 1)
                    for m in range(KF):
                        pe.wait_ge(s_hid, k * KF + (m + 1))
                        i = T.matmul(p_f[:, u], hid[:, u, m * P:(m + 1) * P], w2[:, m], start=(m == 0), stop=(m == KF - 1))
                    i.then_inc(s_f, 1)
                if live(k - 1, NB):
                    q, v = k - 1, 1 - u
                    pe.wait_ge(s_n3, k)
                    for c in range(KD):
                        t = T.transpose(p_t[:, c * P:(c + 1) * P], n3[:, v, c * P:(c + 1) * P], ident[:])
                    t.then_inc(s_t3, 1)
                    pe.wait_ge(s_n3T, k)
                    if reused(q, 2):
                        pe.wait_ge(s_tabled, 2 * (q - 1))
                    if reused(q, 1):
                        pe.wait_ge(s_score, 2 * q)
                    for c in range(KD):
                        T.matmul(p_g[:, v], n3T[:, v, c * P:(c + 1) * P], wg[:, c], start=(c == 0), stop=(c == KD - 1))
                    for c in range(KD):
                        i = T.matmul(p_a[:, 0:W16], n3T[:, v, c * P:(c + 1) * P], wa[:, c].rearrange("p i h -> p (i h)"),
                                     start=(c == 0), stop=(c == KD - 1))
                    i.then_inc(s_g, 1)

            run_steps(pe, NB, 2, 1, step)


def gat_scores(nc, a, g):
    aS, aD = g["aS"], g["aD"]
    sb, ps, sems = g["sb"], g["ps"], g["sems"]
    with ExitStack() as ctx:
        recs = sb(ctx, "recsD", [P, 2, NTILE], I32)
        scratch = sb(ctx, "scratchD", [P, NTILE], I32)
        least = sb(ctx, "leastD", [P, 2 * H])
        top = sb(ctx, "topD", [P, 2 * H])
        s_recs, s_chain, s_least, s_top, s_scores, s_stored = sems(
            ctx, "d_recs d_chain d_least d_top d_scores d_stored")
        block = ctx.enter_context(nc.Block())

        @block.sync
        def _(sp):
            for d in range(2):
                sp.dma_start(recs[:, d], g["slot_recs"][d][0:SLOTS].rearrange("(p t) c -> p (t c)", p=P)).then_inc(s_recs, 16)
            sp.wait_ge(s_scores, 1)
            for d in range(2):
                sp.dma_start(g["gat_rows"][d].rearrange("(t p) c -> p t c", p=P)[:, :, TW:ROW], aS[:, d]).then_inc(s_stored, 16)
            sp.wait_ge(s_stored, 32)

        @block.gpsimd
        def _(pool):
            pool.wait_ge(s_least, 1)
            nc.gpsimd.partition_all_reduce(top[:], least[:], P, bass.bass_isa.ReduceOp.max).then_inc(s_top, 1)

        @block.vector
        def _(dve):
            V = nc.vector
            chain = [0]

            def link(ins):
                chain[0] += 1
                ins.then_inc(s_chain, 1)
                dve.wait_ge(s_chain, chain[0])

            link(V.tensor_reduce(least[:].rearrange("p (d h) -> p d h", d=2), aS[:].rearrange("p d b h -> p d h b"), AX.X, ALU.min))
            V.tensor_scalar(least[:], least[:], -1.0, None, ALU.mult).then_inc(s_least, 1)
            dve.wait_ge(s_recs, 32)
            for d in range(2):
                unpack(V, link, recs[:, d], scratch, g["node_idx"][d], False, g["local"][d])
            dve.wait_ge(s_top, 1)
            for d in range(2):
                shift = top[:, d * H:(d + 1) * H].unsqueeze(1).broadcast_to([P, NB, H])
                link(V.tensor_tensor(aS[:, d], aS[:, d], shift, ALU.add))
                link(V.tensor_tensor(aD[:, d], aD[:, d], shift, ALU.subtract))
            V.memset(scratch[:], 0).then_inc(s_scores, 1)


def gat_edges(nc, a, g):
    d = g["d"]
    acc, local, idx, group_block = g["acc"], g["local"][d], g["node_idx"][d], g["group_block"]
    aD, ident, iota_row = g["aD"], g["ident"], g["iota_row"]
    sb, ps, sems = g["sb"], g["ps"], g["sems"]
    RING, R3, R2 = 6, 3, 2
    AW = NB * TW
    t = "EG"[d]
    with ExitStack() as ctx:
        stage = sb(ctx, "stage" + t, [P, RING, SG], I32)
        rows = [sb(ctx, f"rows{t}{i}", [P, SG, ROW]) for i in range(RING)]
        hot = sb(ctx, "hot" + t, [P, R3, SG, P])
        hotT = sb(ctx, "hotT" + t, [P, R2, SG, P])
        diag = sb(ctx, "diag" + t, [P, R2, SG, H, P])
        peak = sb(ctx, "peak" + t, [P, NB * H])
        shift = sb(ctx, "shift" + t, [P, NB * H])
        fresh = sb(ctx, "fresh" + t, [P, H])
        total = sb(ctx, "total" + t, [P, H])
        node = sb(ctx, "node" + t, [P, R2, 2 * H])
        drop = sb(ctx, "drop" + t, [P, R2, H])
        factor = sb(ctx, "factor" + t, [P, R3, H])
        e = sb(ctx, "e" + t, [P, SG, H])
        weight = sb(ctx, "weight" + t, [P, R2, SG, H])
        msg = sb(ctx, "msg" + t, [P, R2, SG, TW])
        p_T = ps(ctx, "p_T" + t, [P, 512])
        p_x = ps(ctx, "p_x" + t, [P, R2, SG, 512])
        p_n = ps(ctx, "p_n" + t, [P, 512])
        p_s = ps(ctx, "p_s" + t, [P, R2, 512])
        (s_set, s_stage, s_hot, s_T, s_hotT, s_diag, s_x, s_node, s_max, s_drop, s_factor, s_n, s_e, s_weight,
         s_msg, s_sum, s_scaled, s_add, s_own_c, s_own_e) = sems(
            ctx, " ".join(t.lower() + n for n in (
                "_set _stage _hot _T _hotT _diag _x _node _max _drop _factor _n _e _weight _msg _sum _scaled _add "
                "_own_c _own_e").split()))
        s_rows = sems(ctx, " ".join(f"{t.lower()}_rows{i}" for i in range(RING)))
        block = ctx.enter_context(nc.Block())

        @block.gpsimd
        def _(pool):
            def step(k, u, r):
                pool.wait_ge(s_stage, k + 1)
                pool.nop(nofuse=True)
                if reused(k, RING):
                    pool.wait_ge(s_msg, k - (RING - 1))
                    pool.nop(nofuse=True)
                for j in range(SG):
                    nc.gpsimd.indirect_dma_start(
                        out=rows[u][:, j], out_offset=None, in_=g["gat_rows"][d],
                        in_offset=bass.IndirectOffsetOnAxis(ap=stage[:, u, j:j + 1], axis=0)).then_inc(s_rows[u], 16)

            run_steps(pool, NG, RING, 0, step)

        @block.scalar
        def _(act):
            S = nc.scalar
            AHEAD = 3

            def step(k, u, r):
                if live(k, NG):
                    if reused(k, RING):
                        act.wait_ge(s_rows[u], r * (16 * SG))
                    S.copy(stage[:, u], idx[:, bass.ds(k * SG, SG)]).then_inc(s_stage, 1)
                if live(k - AHEAD, NG):
                    q, v = k - AHEAD, (u - AHEAD) % RING
                    act.wait_ge(s_rows[v], (r - (u < AHEAD)) * (16 * SG) + 16 * SG)
                    if reused(q, R2):
                        act.wait_ge(s_x, q - 1)
                    for j in range(SG):
                        for i in range(H):
                            S.activation(diag[:, v % R2, j, i], ident[:], ACT.Copy,
                                         scale=rows[v][:, j, TW + i:TW + i + 1]).then_inc(s_diag, 1)
                    act.wait_ge(s_T, q + 1)
                    if reused(q, R2):
                        act.wait_ge(s_n, q - 1)
                    S.copy(hotT[:, v % R2].rearrange("p j n -> p (j n)"), p_T[:, 0:SG * P]).then_inc(s_hotT, 1)
                if live(k - AHEAD - 1, NG):
                    q, v = k - AHEAD - 1, (u - AHEAD - 1) % RING
                    act.wait_ge(s_drop, q + 1)
                    if reused(q, R3):
                        act.wait_ge(s_scaled, q - 2)
                    S.activation(factor[:, v % R3], drop[:, v % R2], ACT.Exp).then_inc(s_factor, 1)
                if live(k - AHEAD - 2, NG):
                    q, v = k - AHEAD - 2, (u - AHEAD - 2) % RING
                    act.wait_ge(s_e, q + 1)
                    if reused(q, R2):
                        act.wait_ge(s_msg, q - 1)
                    S.activation(weight[:, v % R2], e[:], ACT.Exp).then_inc(s_weight, 1)

            run_steps(act, NG, RING, AHEAD + 2, step)

        @block.vector
        def _(dve):
            V = nc.vector
            NC_, NE = 3, 3

            def own(ins, sem, v):
                ins.then_inc(sem, 1)
                dve.wait_ge(sem, v)

            V.memset(acc[:, d * AW:(d + 1) * AW], 0.0).then_inc(s_add, 1)
            V.memset(peak[:], 0.0).then_inc(s_set, 1)
            V.scalar_tensor_tensor(shift[:], aD[:, d].rearrange("p b h -> p (b h)"), SLOPE,
                                   aD[:, d].rearrange("p b h -> p (b h)"), ALU.mult, ALU.max).then_inc(s_node, 1)
            dve.wait_ge(s_set, 1)

            per_edge = p_n[:, 0:SG * 2 * H].rearrange("p (j c) -> p j c", j=SG)

            def block_of(q):
                return dve.value_load(group_block[0:1, d, bass.ds(q, 1)], min_val=0, max_val=NB - 1)

            def step(k, u, r):
                if live(k, NG):
                    if reused(k, R3):
                        dve.wait_ge(s_sum, k - 2)
                    for j in range(SG):
                        V.tensor_scalar(hot[:, u % R3, j], iota_row[:], local[:, bass.ds(k * SG + j, 1)], None,
                                        ALU.is_equal).then_inc(s_hot, 1)
                if live(k - 2, NG):
                    q, v, w = k - 2, (u - 2) % R2, (u - 2) % RING
                    dve.wait_ge(s_n, q + 1)
                    if reused(q, 1):
                        dve.wait_ge(s_weight, q)
                    own(V.tensor_tensor(e[:], rows[w][:, :, TW:ROW], per_edge[:, :, 0:H], ALU.add), s_own_e, q * NE + 1)
                    own(V.scalar_tensor_tensor(e[:], e[:], SLOPE, e[:], ALU.mult, ALU.max), s_own_e, q * NE + 2)
                    own(V.tensor_tensor(e[:], e[:], per_edge[:, :, H:], ALU.subtract), s_own_e, q * NE + 3)
                    V.tensor_scalar(e[:], e[:], 0.0, None, ALU.min).then_inc(s_e, 1)
                if live(k - 1, NG):
                    q, v = k - 1, (u - 1) % R2
                    b = block_of(q)
                    bh = bass.ds(b * H, H)
                    dve.wait_ge(s_x, q + 1)
                    own(V.tensor_reduce(fresh[:], p_x[:, v].rearrange("p j (h e) -> p h j e", h=H), AX.XY, ALU.max),
                        s_own_c, q * NC_ + 1)
                    dve.wait_ge(s_node, q + 1)
                    own(V.tensor_tensor(peak[:, bh], peak[:, bh], fresh[:], ALU.max), s_own_c, q * NC_ + 2)
                    own(V.tensor_tensor(total[:], peak[:, bh], aD[:, d, bass.ds(b, 1)].rearrange("p o h -> p (o h)"), ALU.add),
                        s_own_c, q * NC_ + 3)
                    if reused(q, R2):
                        dve.wait_ge(s_n, q - 1)
                    dve.nop(nofuse=True)
                    V.tensor_copy(node[:, v, 0:H], aD[:, d, bass.ds(b, 1)].rearrange("p o h -> p (o h)"))
                    V.scalar_tensor_tensor(node[:, v, H:], total[:], SLOPE, total[:], ALU.mult, ALU.max).then_inc(s_max, 1)
                    dve.wait_ge(s_max, q + 1)
                    if reused(q, R2):
                        dve.wait_ge(s_factor, q - 1)
                    own(V.tensor_tensor(drop[:, v], shift[:, bh], node[:, v, H:], ALU.subtract), s_drop, q + 1)
                    dve.nop(nofuse=True)
                    V.tensor_copy(shift[:, bh], node[:, v, H:]).then_inc(s_node, 1)
                if live(k - 3, NG):
                    q, v = k - 3, (u - 3) % R2
                    b = block_of(q)
                    at = acc[:, bass.ds(b * TW + d * AW, TW)]
                    dve.wait_ge(s_factor, q + 1)
                    dve.wait_ge(s_add, q + 1)
                    V.tensor_tensor(at.rearrange("p (h c) -> p h c", h=H), at.rearrange("p (h c) -> p h c", h=H),
                                    factor[:, (u - 3) % R3].unsqueeze(2).broadcast_to([P, H, HW]), ALU.mult).then_inc(s_scaled, 1)
                    dve.wait_ge(s_scaled, q + 1)
                    dve.wait_ge(s_sum, q + 1)
                    V.tensor_tensor(at, at, p_s[:, v, 0:TW], ALU.add).then_inc(s_add, 1)
                if live(k - 2, NG):
                    q, v, w = k - 2, (u - 2) % R2, (u - 2) % RING
                    dve.wait_ge(s_weight, q + 1)
                    if reused(q, R2):
                        dve.wait_ge(s_sum, q - 1)
                    V.tensor_tensor(msg[:, v].rearrange("p j (h c) -> p j h c", h=H),
                                    rows[w][:, :, 0:TW].rearrange("p j (h c) -> p j h c", h=H),
                                    weight[:, v].unsqueeze(3).broadcast_to([P, SG, H, HW]), ALU.mult).then_inc(s_msg, 1)

            run_steps(dve, NG, RING, 3, step)

        @block.tensor
        def _(pe):
            T = nc.tensor

            def step(k, u, r):
                if live(k, NG):
                    v = u % R2
                    pe.wait_ge(s_hot, k * SG + SG)
                    if reused(k, 1):
                        pe.wait_ge(s_hotT, k)
                    for j in range(SG):
                        i = T.transpose(p_T[:, j * P:(j + 1) * P], hot[:, u % R3, j], ident[:])
                    i.then_inc(s_T, 1)
                    pe.wait_ge(s_diag, k * (SG * H) + SG * H)
                    if reused(k, R2):
                        pe.wait_ge(s_own_c, (k - 2) * 3 + 1)
                    for j in range(SG):
                        i = T.matmul(p_x[:, v, j], hot[:, u % R3, j], diag[:, v, j].rearrange("p h e -> p (h e)"),
                                     start=True, stop=True)
                    i.then_inc(s_x, 1)
                if live(k - 1, NG):
                    q, v = k - 1, (u - 1) % R2
                    pe.wait_ge(s_hotT, q + 1)
                    pe.wait_ge(s_max, q + 1)
                    if reused(q, 1):
                        pe.wait_ge(s_own_e, (q - 1) * 3 + 3)
                    for j in range(SG):
                        i = T.matmul(p_n[:, j * 2 * H:(j + 1) * 2 * H], hotT[:, v, j], node[:, v],
                                     start=True, stop=True)
                    i.then_inc(s_n, 1)
                if live(k - 2, NG):
                    q, v, h3 = k - 2, (u - 2) % R2, (u - 2) % R3
                    pe.wait_ge(s_msg, q + 1)
                    if reused(q, R2):
                        pe.wait_ge(s_add, q)
                    for j in range(SG):
                        i = T.matmul(p_s[:, v, 0:TW], hot[:, h3, j], msg[:, v, j], start=(j == 0), stop=(j == SG - 1))
                    i.then_inc(s_sum, 1)

            run_steps(pe, NG, RING, 2, step)


def fuse(nc, a, g):
    acc, ident, ones, ones_last, eps_col = g["acc"], g["ident"], g["ones"], g["ones_last"], g["eps_col"]
    sb, ps, sems = g["sb"], g["ps"], g["sems"]
    HC = H * C
    sides = acc[:, 0:2 * NB * TW].rearrange("p (d w) -> p d w", d=2)
    with ExitStack() as ctx:
        wf = sb(ctx, "wfF", [P, KD, D])
        rows = {n: sb(ctx, f"rowF_{n}", [P, D]) for n in ("b_fuse", "bn_gamma", "bn_beta")}
        bias = sb(ctx, "biasF", [P, 2, HC])
        inv = sb(ctx, "invF", [P, 2, H])
        comb = sb(ctx, "combF", [P, 2, 2, HC])
        combT = sb(ctx, "combTF", [P, 2, D])
        mean = sb(ctx, "meanF", [P, 2, HC])
        scale = sb(ctx, "scaleF", [P, 2, HC])
        square = sb(ctx, "squareF", [P, 2, D])
        mid = sb(ctx, "midF", [P, 2, D])
        y = sb(ctx, "yF", [P, 2, 2, HC])
        p_t = ps(ctx, "p_tF", [P, 2, 512])
        p_f = ps(ctx, "p_fF", [P, 2, 512])
        p_sum = ps(ctx, "p_sumF", [P, 2, 512])
        (s_w, s_own, s_comb, s_t, s_combT, s_f, s_fused, s_summed, s_mean, s_diff, s_square, s_squared, s_sd,
         s_chain, s_scale, s_own3, s_y) = sems(
            ctx, "f_w f_own f_comb f_t f_combT f_f f_fused f_summed f_mean f_diff f_square f_squared f_sd "
                 "f_chain f_scale f_own3 f_y")
        s_mid, s_out = sems(ctx, "f_mid0 f_mid1"), sems(ctx, "f_out0 f_out1")
        block = ctx.enter_context(nc.Block())

        def fused(k):
            return sides[:, :, bass.ds(k * TW, HC)]

        @block.sync
        def _(sp):
            sp.dma_start(wf[:], a["L1_gnn_W_fuse"].rearrange("(k p) f -> p k f", p=P)).then_inc(s_w, 16)
            for n, ap in rows.items():
                sp.dma_start(ap[:], a["L1_gnn_" + n].partition_broadcast(P)).then_inc(s_w, 16)
            for d, t in enumerate("fb"):
                sp.dma_start(bias[:, d], a["L1_gnn_bias_" + t].partition_broadcast(P)).then_inc(s_w, 16)

            def step(k, u, r):
                if reused(k, 2):
                    sp.wait_ge(s_y, k - 1)
                sp.dma_start(mid[:, u], x_rows(g["mid_rows"], k)).then_inc(s_mid[u], 16)

            run_steps(sp, NB, 2, 0, step)

        @block.vector
        def _(dve):
            V = nc.vector
            chain = [0]

            def link(ins):
                chain[0] += 1
                ins.then_inc(s_chain, 1)
                dve.wait_ge(s_chain, chain[0])

            NOWN = 3

            def own(ins, k, n):
                ins.then_inc(s_own, 1)
                dve.wait_ge(s_own, k * NOWN + n)

            dve.wait_ge(s_w, 16 * 6)

            def combine(k, u, r):
                if live(k, NB):
                    heads = sides[:, :, bass.ds(k * TW, TW)].rearrange("p d (h c) -> p d h c", h=H)
                    own(V.tensor_scalar(inv[:], heads[:, :, :, C], 1e-16, None, ALU.add), k, 1)
                    own(V.reciprocal(inv[:], inv[:]), k, 2)
                    if reused(k, 2):
                        dve.wait_ge(s_t, k - 1)
                    for d in range(2):
                        i = V.tensor_tensor(comb[:, u, d].rearrange("p (h c) -> p h c", h=H), heads[:, d, :, 0:C],
                                            inv[:, d].unsqueeze(2).broadcast_to([P, H, C]), ALU.mult)
                    own(i, k, 3)
                    V.tensor_tensor(comb[:, u], comb[:, u], bias[:], ALU.add).then_inc(s_comb, 1)
                if live(k - 1, NB):
                    q, v = k - 1, 1 - u
                    dve.wait_ge(s_f, k)
                    V.tensor_tensor(fused(q), p_f[:, v].rearrange("p (d c) -> p d c", d=2),
                                    rows["b_fuse"][:].rearrange("p (d c) -> p d c", d=2), ALU.add).then_inc(s_fused, 1)

            run_steps(dve, NB, 2, 1, combine)
            dve.wait_ge(s_summed, NB)
            link(V.tensor_scalar(mean[:], p_sum[:, 0].rearrange("p (d c) -> p d c", d=2), 1.0 / N, None, ALU.mult))

            def centre(k, u, r):
                V.tensor_tensor(fused(k), fused(k), mean[:], ALU.subtract).then_inc(s_diff, 1)

            run_steps(dve, NB, 2, 0, centre)
            dve.wait_ge(s_sd, 1)
            link(V.reciprocal(scale[:], scale[:]))
            link(V.tensor_tensor(scale[:], scale[:], rows["bn_gamma"][:].rearrange("p (d c) -> p d c", d=2), ALU.mult))

            def finish(k, u, r):
                if reused(k, 2):
                    dve.wait_ge(s_out[u], r * 16)
                V.tensor_tensor(y[:, u], fused(k), scale[:], ALU.mult).then_inc(s_own3, 1)
                dve.wait_ge(s_own3, 2 * k + 1)
                V.tensor_tensor(y[:, u], y[:, u], rows["bn_beta"][:].rearrange("p (d c) -> p d c", d=2),
                                ALU.add).then_inc(s_own3, 1)
                dve.wait_ge(s_own3, 2 * k + 2)
                dve.wait_ge(s_mid[u], r * 16 + 16)
                V.scalar_tensor_tensor(y[:, u], y[:, u], 0.0, mid[:, u].rearrange("p (d c) -> p d c", d=2),
                                       ALU.max, ALU.add).then_inc(s_y, 1)

            run_steps(dve, NB, 2, 0, finish)

        @block.scalar
        def _(act):
            S = nc.scalar

            def copy(k, u, r):
                act.wait_ge(s_t, k + 1)
                if reused(k, 2):
                    act.wait_ge(s_f, k - 1)
                S.copy(combT[:, u], p_t[:, u]).then_inc(s_combT, 1)

            run_steps(act, NB, 2, 0, copy)

            def squares(k, u, r):
                act.wait_ge(s_diff, k + 1)
                if reused(k, 2):
                    act.wait_ge(s_squared, k - 1)
                S.activation(square[:, u].rearrange("p (d c) -> p d c", d=2), fused(k), ACT.Square).then_inc(s_square, 1)

            run_steps(act, NB, 2, 0, squares)
            act.wait_ge(s_squared, NB)
            S.activation(scale[:], p_sum[:, 1].rearrange("p (d c) -> p d c", d=2), ACT.Sqrt, bias=eps_col[:],
                         scale=1.0 / N).then_inc(s_sd, 1)

            def store(k, u, r):
                act.wait_ge(s_y, k + 1)
                act.dma_start(x_rows(a["out"], k), y[:, u].rearrange("p d c -> p (d c)")).then_inc(s_out[u], 16)

            run_steps(act, NB, 2, 0, store)
            for u in range(2):
                act.wait_ge(s_out[u], 16 * len(range(u, NB, 2)))

        @block.tensor
        def _(pe):
            T = nc.tensor
            pe.wait_ge(s_w, 16 * 6)

            def last(k):
                return isinstance(k, int) and k == NB - 1

            def first(k):
                return isinstance(k, int) and k == 0

            def step(k, u, r):
                if live(k, NB):
                    pe.wait_ge(s_comb, k + 1)
                    if reused(k, 2):
                        pe.wait_ge(s_combT, k - 1)
                    for c in range(KD):
                        t = T.transpose(p_t[:, u, c * P:(c + 1) * P], comb[:, u].rearrange("p d c -> p (d c)")[:, c * P:(c + 1) * P],
                                        ident[:])
                    t.then_inc(s_t, 1)
                    pe.wait_ge(s_combT, k + 1)
                    if reused(k, 2):
                        pe.wait_ge(s_fused, k - 1)
                    for c in range(KD):
                        m = T.matmul(p_f[:, u], combT[:, u, c * P:(c + 1) * P], wf[:, c], start=(c == 0), stop=(c == KD - 1))
                    m.then_inc(s_f, 1)
                if live(k - 1, NB):
                    q = k - 1
                    pe.wait_ge(s_fused, k)
                    m = T.matmul(p_sum[:, 0], (ones_last if last(q) else ones)[:], fused(q), start=first(q), stop=last(q))
                    m.then_inc(s_summed, 1)

            run_steps(pe, NB, 2, 1, step)

            def var(k, u, r):
                pe.wait_ge(s_square, k + 1)
                T.matmul(p_sum[:, 1], (ones_last if last(k) else ones)[:], square[:, u],
                         start=first(k), stop=last(k)).then_inc(s_squared, 1)

            run_steps(pe, NB, 2, 0, var)


WEIGHTS = ["L0_gnn_self_W", "L0_gnn_self_b", "L0_gnn_rel_W", "L0_gnn_rel_b", "L0_gnn_ln1_w", "L0_gnn_ln1_b",
           "L0_gnn_W1", "L0_gnn_b1", "L0_gnn_W2", "L0_gnn_b2", "L0_gnn_ln2_w", "L0_gnn_ln2_b", "L1_gnn_W_f",
           "L1_gnn_att_src_f", "L1_gnn_att_dst_f", "L1_gnn_bias_f", "L1_gnn_W_b", "L1_gnn_att_src_b",
           "L1_gnn_att_dst_b", "L1_gnn_bias_b", "L1_gnn_W_fuse", "L1_gnn_b_fuse", "L1_gnn_bn_gamma", "L1_gnn_bn_beta"]


def kernel(**inputs):
    import numpy as _np
    import concourse.bacc as _bacc
    from concourse.bass_utils import run_bass_kernel_spmd as _run

    arrays = {}
    arrays["x"] = _np.zeros((NPAD, D), _np.float32)
    arrays["x"][:N] = _np.asarray(inputs["x"])
    for name, fill in (("src", NPAD), ("dst", NPAD), ("edge_type_4", 0)):
        padded = _np.full(P * EC, fill, _np.int32)
        padded[:E] = _np.asarray(inputs[name])
        arrays[name] = padded.reshape(P, EC)
    for name in WEIGHTS:
        arrays[name] = _np.ascontiguousarray(inputs[name])
    arrays["L0_gnn_b1"] = _np.ascontiguousarray(arrays["L0_gnn_b1"].reshape(KF, P).T)

    nc = _bacc.Bacc("TRN2", target_bir_lowering=False, num_devices=1)
    a = {"scratch_kind": "Internal"}
    for name, v in arrays.items():
        a[name] = nc.dram_tensor("in_" + name, v.shape, mybir.dt.from_np(v.dtype), kind="ExternalInput").ap()
    a["out"] = nc.dram_tensor("out_0", (NPAD, D), F32, kind="ExternalOutput").ap()
    program(nc, a)
    r = _run(nc, [{"in_" + n: v for n, v in arrays.items()}], core_ids=[0])
    return r.results[0]["out_0"][:N]
```
